# Optimizing a Trainium2 kernel written in Bass

```python
import numpy as np
import jax
import jax.numpy as jnp

def _softmax(x, axis=-1):
    return jax.nn.softmax(x, axis=axis)

def _gelu(x):
    return jax.nn.gelu(x, approximate=True)

def _silu(x):
    return jax.nn.silu(x)

def _sigmoid(x):
    return jax.nn.sigmoid(x)

def _layernorm(x, axis=-1, eps=1e-05):
    m = jnp.mean(x, axis=axis, keepdims=True)
    v = jnp.var(x, axis=axis, keepdims=True)
    return (x - m) / jnp.sqrt(v + eps)

def _scatter_add(tgt, idx, src, axis=0):
    return tgt.at[idx].add(src)

def _segment_sum(src, seg, n):
    return jax.ops.segment_sum(src, seg, n)
kernel_name = 'mk_gnn_preln_d1_gnn_r8_7db78e'

def setup_inputs(seed: int=0):
    np.random.seed(seed)
    _w = jnp.asarray

    def _rec_inputs():
        import jax
        import jax.numpy as jnp
        _gk = jax.random.key(seed)
        x = -0.0005121 + 1.001 * jax.random.normal(jax.random.fold_in(_gk, 1), (6250, 64), jnp.float32)
        src = jax.random.randint(jax.random.fold_in(_gk, 2), (200000,), 0, 6250, jnp.int32)
        dst = jax.random.randint(jax.random.fold_in(_gk, 3), (200000,), 0, 6250, jnp.int32)
        _o = jnp.argsort(dst, stable=True)
        src = src[_o]
        dst = dst[_o]
        edge_attr_64 = -9.77346e-05 + 0.999888 * jax.random.normal(jax.random.fold_in(_gk, 11), (200000, 64), jnp.float32)
        return (x, src, dst, edge_attr_64)
    x, src, dst, edge_attr_64 = _rec_inputs()

    def _L0_gnn_setup():
        import jax, jax.numpy as jnp
        import numpy as np
        N = 6250
        E = 100000
        D = 64
        L = 3
        LN_EPS = 1e-05

        def _transformer_conv(x, src, dst, edge_attr, Wq, bq, Wk, bk, Wv, bv, We, Ws, bs):
            q = x @ Wq + bq
            k = x @ Wk + bk
            v = x @ Wv + bv
            e = edge_attr @ We
            kj = k[src] + e
            alpha = jnp.sum(q[dst] * kj, axis=-1) / jnp.sqrt(jnp.float32(D))
            amax = jax.ops.segment_max(alpha, dst, num_segments=N)
            p = jnp.exp(alpha - amax[dst])
            denom = jax.ops.segment_sum(p, dst, num_segments=N)
            w = p / denom[dst]
            msg = (v[src] + e) * w[:, None]
            agg = jax.ops.segment_sum(msg, dst, num_segments=N)
            return agg + x @ Ws + bs

        def _layer_norm(x, gamma, beta):
            mu = jnp.mean(x, axis=-1, keepdims=True)
            var = jnp.mean(jnp.square(x - mu), axis=-1, keepdims=True)
            return (x - mu) * jax.lax.rsqrt(var + LN_EPS) * gamma + beta
        key = jax.random.key(seed)
        ks = jax.random.split(key, 16)
        s = 1.0 / np.sqrt(D)
        node_attr = jax.random.normal(ks[0], (N, D), dtype=jnp.float32)
        edge_attr = jax.random.normal(ks[1], (E, D), dtype=jnp.float32)
        edge_index = jax.random.randint(ks[2], (2, E), 0, N, dtype=jnp.int32)
        mk = lambda k: jax.random.normal(k, (L, D, D), dtype=jnp.float32) * s
        return {'node_attr': node_attr, 'edge_index': edge_index, 'edge_attr': edge_attr, 'Wq': mk(ks[3]), 'bq': jnp.zeros((L, D), jnp.float32), 'Wk': mk(ks[4]), 'bk': jnp.zeros((L, D), jnp.float32), 'Wv': mk(ks[5]), 'bv': jnp.zeros((L, D), jnp.float32), 'We': mk(ks[6]), 'Ws': mk(ks[7]), 'bs': jnp.zeros((L, D), jnp.float32), 'ln_gamma': jnp.ones((L - 1, D), jnp.float32), 'ln_beta': jnp.zeros((L - 1, D), jnp.float32)}
    _L0_gnn_all = _L0_gnn_setup()
    _L0_gnn_in = {k: v for k, v in _L0_gnn_all.items() if k in ('Wq', 'bq', 'Wk', 'bk', 'Wv', 'bv', 'We', 'Ws', 'bs', 'ln_gamma', 'ln_beta')}
    del _L0_gnn_all
    return {'x': x, 'src': src, 'dst': dst, 'edge_attr_64': edge_attr_64, 'L0_gnn_Wq': _L0_gnn_in['Wq'], 'L0_gnn_bq': _L0_gnn_in['bq'], 'L0_gnn_Wk': _L0_gnn_in['Wk'], 'L0_gnn_bk': _L0_gnn_in['bk'], 'L0_gnn_Wv': _L0_gnn_in['Wv'], 'L0_gnn_bv': _L0_gnn_in['bv'], 'L0_gnn_We': _L0_gnn_in['We'], 'L0_gnn_Ws': _L0_gnn_in['Ws'], 'L0_gnn_bs': _L0_gnn_in['bs'], 'L0_gnn_ln_gamma': _L0_gnn_in['ln_gamma'], 'L0_gnn_ln_beta': _L0_gnn_in['ln_beta']}

def reference(x, src, dst, edge_attr_64, L0_gnn_Wq, L0_gnn_bq, L0_gnn_Wk, L0_gnn_bk, L0_gnn_Wv, L0_gnn_bv, L0_gnn_We, L0_gnn_Ws, L0_gnn_bs, L0_gnn_ln_gamma, L0_gnn_ln_beta):
    import jax
    import jax.numpy as jnp

    def _L0_gnn_ref(node_attr, edge_index, edge_attr, Wq, bq, Wk, bk, Wv, bv, We, Ws, bs, ln_gamma, ln_beta):
        import jax, jax.numpy as jnp
        import numpy as np
        N = 6250
        E = 100000
        D = 64
        L = 3
        LN_EPS = 1e-05

        def _transformer_conv(x, src, dst, edge_attr, Wq, bq, Wk, bk, Wv, bv, We, Ws, bs):
            q = x @ Wq + bq
            k = x @ Wk + bk
            v = x @ Wv + bv
            e = edge_attr @ We
            kj = k[src] + e
            alpha = jnp.sum(q[dst] * kj, axis=-1) / jnp.sqrt(jnp.float32(D))
            amax = jax.ops.segment_max(alpha, dst, num_segments=N)
            p = jnp.exp(alpha - amax[dst])
            denom = jax.ops.segment_sum(p, dst, num_segments=N)
            w = p / denom[dst]
            msg = (v[src] + e) * w[:, None]
            agg = jax.ops.segment_sum(msg, dst, num_segments=N)
            return agg + x @ Ws + bs

        def _layer_norm(x, gamma, beta):
            mu = jnp.mean(x, axis=-1, keepdims=True)
            var = jnp.mean(jnp.square(x - mu), axis=-1, keepdims=True)
            return (x - mu) * jax.lax.rsqrt(var + LN_EPS) * gamma + beta
        src, dst = (edge_index[0], edge_index[1])
        x = node_attr
        for i in range(L):
            x = _transformer_conv(x, src, dst, edge_attr, Wq[i], bq[i], Wk[i], bk[i], Wv[i], bv[i], We[i], Ws[i], bs[i])
            x = jax.nn.relu(x)
            if i < L - 1:
                x = _layer_norm(x, ln_gamma[i], ln_beta[i])
        return jax.nn.log_softmax(x, axis=1)
    edge_index = jnp.stack([src, dst])
    h = jnp.maximum(_layernorm(x, axis=-1), 0.0)
    x = x + _L0_gnn_ref(h, edge_index, edge_attr_64, L0_gnn_Wq, L0_gnn_bq, L0_gnn_Wk, L0_gnn_bk, L0_gnn_Wv, L0_gnn_bv, L0_gnn_We, L0_gnn_Ws, L0_gnn_bs, L0_gnn_ln_gamma, L0_gnn_ln_beta)
    return x

_drawn_inputs = setup_inputs


def setup_inputs(seed=0):
    import zlib

    import numpy as np

    out = dict(_drawn_inputs(seed))
    spreads = {'L0_gnn_bq': (0.0, 0.492),
     'L0_gnn_bk': (0.0, 0.8),
     'L0_gnn_bv': (0.0, 0.1),
     'L0_gnn_bs': (0.0, 0.1),
     'L0_gnn_ln_gamma': (1.0, 0.2),
     'L0_gnn_ln_beta': (0.0, 0.1)}
    factors = {}
    for name, (base, spread) in spreads.items():
        noise = np.random.default_rng([zlib.crc32(name.encode()), seed]).standard_normal(out[name].shape)
        drawn = base * np.exp(spread * noise) if base else spread * noise
        out[name] = jnp.asarray(drawn.astype(out[name].dtype))
    for name, factor in factors.items():
        out[name] = (out[name] * factor).astype(out[name].dtype)
    return out
```

```python
from contextlib import ExitStack

import numpy as np

import concourse.bass as bass
from concourse import mybir

F32 = mybir.dt.float32
I32 = mybir.dt.int32
ALU = mybir.AluOpType
ACT = mybir.ActivationFunctionType
AX = mybir.AxisListType.X

N, E, D, LAYERS = 6250, 200000, 64, 3
P = 128
EPS = 1e-5
BLOCKS = -(-N // P)
NPAD = BLOCKS * P
TILES = 4
C = TILES * P
LOG_C = C.bit_length() - 1
SLOTS = 4
STEPS = -(-(E // C + BLOCKS) // SLOTS) * SLOTS
ROUNDS = STEPS // SLOTS
SAMPLE = 32
EPAD = P * BLOCKS * SAMPLE
FAR = 1 << 20
ZW = 2 * D + 1
HW = D + 2
NG = 7
GROUPS = BLOCKS // NG
LOW = -1e30
NORM_OPS, MEAN_OPS = 7, 1
LOWER = -1e35
assert EPAD >= E + C and GROUPS * NG == BLOCKS


def program(nc, x, ends, dst_rows, edge_attr, wq_t, w_keys, w_values, w_skip, gamma, beta, out):
    h_table = nc.dram_tensor("h_table", (NPAD, D), F32).ap()

    with ExitStack() as ctx:
        def sb(name, shape, dt=F32):
            return ctx.enter_context(nc.sbuf_tensor(name, shape, dt))

        def sem(name):
            return ctx.enter_context(nc.semaphore(name))

        iota_i = sb("iota_i", [P, STEPS], I32)
        iota_row = sb("iota_row", [P, STEPS])
        iota_pi = sb("iota_pi", [P, 1], I32)
        iota_p = sb("iota_p", [P, 1])
        ident = sb("ident", [P, P])
        ones = sb("ones", [P, 1])
        dst_all = sb("dst_all", [P, BLOCKS * SAMPLE], I32)
        below = sb("below", [P, BLOCKS + 1, BLOCKS])
        limits = sb("limits", [P, BLOCKS + 1])
        limit_p = sb("limit_p", [P, 1])
        coarse = sb("coarse", [P, BLOCKS + 1])
        row_f = sb("row_f", [P, 1])
        row_i = sb("row_i", [P, 1], I32)
        window = sb("window", [P, SAMPLE], I32)
        fine = sb("fine", [P, SAMPLE])
        fine_n = sb("fine_n", [P, 1])
        start_col = sb("start_col", [P, 1])
        shift_a = sb("shift_a", [P, P])
        shift_b = sb("shift_b", [P, P])
        next_less = sb("next_less", [P, P])
        less_prev = sb("less_prev", [P, P])
        earlier = sb("earlier", [P, P])
        n_edges = sb("n_edges", [P, 1])
        n_i = sb("n_i", [P, 1], I32)
        n_shifted = sb("n_shifted", [P, 1], I32)
        n_steps = sb("n_steps", [P, 1])
        first_step = sb("first_step", [P, 1])
        base = sb("base", [P, 1])
        base_step = sb("base_step", [P, 1])
        begun = sb("begun", [P, STEPS])
        is_later = sb("is_later", [P, P])
        at_f = sb("at_f", [1, STEPS])
        at_c = sb("at_c", [1, STEPS])
        step_edge = sb("step_edge", [1, STEPS], I32)
        step_block = sb("step_block", [1, STEPS], I32)
        node_0 = sb("node_0", [P, STEPS])
        same = sb("same", [P, STEPS])
        cap = sb("cap", [P, STEPS])
        pair = sb("pair", [P, SLOTS, TILES * 2], I32)
        z = sb("z", [P, SLOTS, TILES, ZW])
        qq = sb("qq", [P, SLOTS, ZW])
        rel = sb("rel", [P, SLOTS, TILES])
        alpha = sb("alpha", [P, SLOTS, TILES])
        less_max = sb("less_max", [P, SLOTS, TILES])
        prob = sb("prob", [P, SLOTS, TILES])
        at_node = sb("at_node", [P, 2, C])
        barred = sb("barred", [P, 2, C])
        weigh = sb("weigh", [P, 2, TILES, P])
        scratch_z = sb("scratch_z", [P, TILES, ZW])
        scratch_c = sb("scratch_c", [P, C])
        max_before = sb("max_before", [P, SLOTS])
        max_step = sb("max_step", [P, SLOTS])
        max_now = sb("max_now", [P, SLOTS])
        max_fell = sb("max_fell", [P, SLOTS])
        rescale = sb("rescale", [P, SLOTS])
        total = sb("total", [P, SLOTS, ZW])
        x_in = sb("x_in", [P, BLOCKS, D])
        hx = sb("hx", [P, BLOCKS, HW])
        new = sb("new", [P, BLOCKS, D])
        work = sb("work", [P, BLOCKS, D])
        stat = sb("stat", [P, BLOCKS])
        spread = sb("spread", [P, BLOCKS])
        deviation = sb("deviation", [P, BLOCKS])
        inverse = sb("inverse", [P, BLOCKS])
        u_all = sb("u_all", [P, BLOCKS, ZW])
        mean_g = sb("mean_g", [P, NG, 2 * D])
        hx_g = sb("hx_g", [P, NG, HW])
        exps = sb("exps", [P, BLOCKS, D])
        qq_all = sb("qq_all", [P, BLOCKS, ZW])
        zt = sb("zt", [P, NG, P])
        ht = sb("ht", [HW, NG, P])
        wq_sb = sb("wq_sb", [D, D + 1])
        wk_sb = sb("wk_sb", [D, ZW])
        wv_sb = sb("wv_sb", [2 * D, D])
        ws_sb = sb("ws_sb", [HW, D])
        wqk = sb("wqk", [D + 1, ZW])
        gamma_sb = sb("gamma_sb", [P, D])
        beta_sb = sb("beta_sb", [P, D])

        bank = [ctx.enter_context(nc.psum_tensor(f"bank{i}", [P, 512], F32)) for i in range(8)]
        dst_row, alpha_row = bank[0], bank[1]
        q_edge = [bank[2], bank[3]]
        sums = [bank[4], bank[5]]
        edge_max = bank[6]

        s_x, s_dst, s_w, s_norm, weights_in, s_iota = map(sem, (
            "s_x", "s_dst", "s_w", "s_norm", "weights_in", "s_iota"))
        prep_dve, prep_dve2, coarse_ready, pe_prep, row_ready, s_window = map(sem, (
            "prep_dve", "prep_dve2", "coarse_ready", "pe_prep", "row_ready", "s_window"))
        start_ready, n_steps_ready, base_ready, begun_ready, base_step_ready, s_table = map(sem, (
            "start_ready", "n_steps_ready", "base_ready", "begun_ready", "base_step_ready", "s_table"))
        rel_ready, dst_row_ready, at_node_ready, barred_ready, q_edge_ready, alpha_ready = map(sem, (
            "rel_ready", "dst_row_ready", "at_node_ready", "barred_ready", "q_edge_ready", "alpha_ready"))
        alpha_row_ready, max_before_ready, max_step_ready, max_now_ready, max_fell_ready, rescale_ready = map(sem, (
            "alpha_row_ready", "max_before_ready", "max_step_ready", "max_now_ready", "max_fell_ready", "rescale_ready"))
        edge_max_ready, less_max_ready, prob_ready, weigh_ready, sums_ready, total_ready = map(sem, (
            "edge_max_ready", "less_max_ready", "prob_ready", "weigh_ready", "sums_ready", "total_ready"))
        total_kept, norm_dve, variance_ready, deviation_ready, h_ready, h_stored = map(sem, (
            "total_kept", "norm_dve", "variance_ready", "deviation_ready", "h_ready", "h_stored"))
        wqk_done, wqk_ready, qt_done, qt_ready, qq_done, qq_ready = map(sem, (
            "wqk_done", "wqk_ready", "qt_done", "qt_ready", "qq_done", "qq_ready"))
        mean_dve, mean_ready, weights_ready, hx_g_ready, hx_h_ready, zt_done, zt_ready, ht_done, ht_ready = map(sem, (
            "mean_dve", "mean_ready", "weights_ready", "hx_g_ready", "hx_h_ready", "zt_done", "zt_ready", "ht_done", "ht_ready"))
        new_done, new_ready, last_dve, shifted_ready, exp_ready, sum_ready = map(sem, (
            "new_done", "new_ready", "last_dve", "shifted_ready", "exp_ready", "sum_ready"))
        log_ready, out_ready, s_out = map(sem, (
            "log_ready", "out_ready", "s_out"))
        pair_loaded = [sem(f"pair_loaded{u}") for u in range(SLOTS)]
        edge_loaded = [sem(f"edge_loaded{u}") for u in range(SLOTS)]
        h_loaded = [sem(f"h_loaded{u}") for u in range(SLOTS)]
        passed_sp, passed_pool, passed_dve, passed_pe = map(sem, ("passed_sp", "passed_pool", "passed_dve", "passed_pe"))
        block = ctx.enter_context(nc.Block())

        def node_view(t):
            return t.rearrange("(b p) d -> p b d", p=P)

        @block.sync
        def _(sp):
            sp.dma_start(dst_all[:, :], dst_rows.rearrange("(p k) c -> p (k c)", p=P)).then_inc(s_dst, 16)
            sp.dma_start(x_in[:, :, :], node_view(x)).then_inc(s_x, 16)

            def load_weights(l):
                sp.dma_start(wq_sb[:, :], wq_t[bass.ds(l, 1), :, :].rearrange("o a b -> (o a) b")).then_inc(weights_in, 16)
                sp.dma_start(wk_sb[:, :], w_keys[bass.ds(l, 1), :, :].rearrange("o a b -> (o a) b")).then_inc(weights_in, 16)

            def load_out_weights(l):
                sp.dma_start(wv_sb[:, :], w_values[bass.ds(l, 1), :, :].rearrange("o a b -> (o a) b")).then_inc(s_w, 16)
                sp.dma_start(ws_sb[:, :], w_skip[bass.ds(l, 1), :, :].rearrange("o a b -> (o a) b")).then_inc(s_w, 16)

            def load_norm(l):
                sp.dma_start(gamma_sb[:, :], gamma[bass.ds(l, 1), :].partition_broadcast(P)).then_inc(s_norm, 16)
                sp.dma_start(beta_sb[:, :], beta[bass.ds(l, 1), :].partition_broadcast(P)).then_inc(s_norm, 16)

            def store_h(l):
                sp.wait_ge(h_ready, l + 1)
                sp.dma_start(node_view(h_table), hx[:, :, 0:D]).then_inc(h_stored, 16)
                sp.wait_ge(qq_ready, (l + 1) * GROUPS)
                sp.sem_inc(passed_sp, 1)
                sp.wait_ge(h_stored, (l + 1) * 16)
                sp.sem_inc(passed_sp, 1)

            def load_step(s, u):
                at = sp.value_load(step_edge[0:1, bass.ds(s, 1)], min_val=0, max_val=E)
                b = sp.value_load(step_block[0:1, bass.ds(s, 1)], min_val=0, max_val=BLOCKS - 1)
                sp.dma_start(pair[:, u, :], ends[bass.ds(at, C), :].rearrange("(p k) o -> p (k o)", p=P))\
                    .then_inc(pair_loaded[u], 16)
                sp.dma_start(z[:, u, :, D:2 * D], edge_attr[bass.ds(at, C), :].rearrange("(p k) d -> p k d", p=P))\
                    .then_inc(edge_loaded[u], 16)
                sp.dma_start(qq[:, u, :], qq_all[:, bass.ds(b, 1), :].rearrange("p o d -> p (o d)"))\
                    .then_inc(edge_loaded[u], 16)

            def keep_total(l, s, u):
                b = sp.value_load(step_block[0:1, bass.ds(s, 1)], min_val=0, max_val=BLOCKS - 1)
                sp.wait_ge(total_ready, l * STEPS + s + 2)
                sp.dma_start(u_all[:, bass.ds(b, 1), :].rearrange("p o d -> p (o d)"), total[:, u, :])\
                    .then_inc(total_kept, 16)

            def edge_phase(l):
                for u in range(SLOTS):
                    load_step(u, u)
                with sp.Fori(0, ROUNDS - 1) as r:
                    for u in range(SLOTS):
                        s = r * SLOTS + u
                        keep_total(l, s, u)
                        load_step(s + SLOTS, u)
                        sp.wait_ge(total_kept, (l * STEPS + s + 1) * 16)
                        sp.sem_inc(passed_sp, 1)
                for u in range(SLOTS):
                    s = STEPS - SLOTS + u
                    keep_total(l, s, u)
                    sp.wait_ge(total_kept, (l * STEPS + s + 1) * 16)
                    sp.sem_inc(passed_sp, 1)

            load_weights(0)
            sp.wait_ge(s_table, 1)
            store_h(0)
            with sp.Fori(0, LAYERS - 1) as l:
                load_out_weights(l)
                load_norm(l)
                sp.wait_ge(wqk_ready, l + 1)
                sp.sem_inc(passed_sp, 1)
                load_weights(l + 1)
                edge_phase(l)
                store_h(l + 1)
            load_out_weights(LAYERS - 1)
            edge_phase(LAYERS - 1)
            sp.wait_ge(out_ready, 1)
            whole = N // P
            sp.dma_start(out[0:whole * P, :].rearrange("(b p) d -> p b d", p=P), work[:, 0:whole, :]).then_inc(s_out, 16)
            sp.dma_start(out[whole * P:N, :], work[0:N - whole * P, whole, :]).then_inc(s_out, 16)
            sp.wait_ge(s_out, 32)

        @block.gpsimd
        def _(pool):
            pool.iota(iota_i[:, :], [[1, STEPS]], base=0, channel_multiplier=0).then_inc(s_iota, 1)
            pool.iota(iota_pi[:, :], [[0, 1]], base=0, channel_multiplier=1).then_inc(s_iota, 1)
            pool.wait_ge(row_ready, 1)
            pool.indirect_dma_start(window[0:BLOCKS + 1, :], None, dst_rows[:, :],
                                    bass.IndirectOffsetOnAxis(ap=row_i[0:BLOCKS + 1, 0:1], axis=0)).then_inc(s_window, 16)

            with pool.Fori(0, LAYERS * ROUNDS) as g:
                for u in range(SLOTS):
                    pool.wait_ge(pair_loaded[u], (g + 1) * 16)
                    pool.sem_inc(passed_pool, 1)
                    for j in range(TILES):
                        pool.indirect_dma_start(z[:, u, j, 0:D], None, h_table[:, :],
                                                bass.IndirectOffsetOnAxis(ap=pair[:, u, 2 * j:2 * j + 1], axis=0))\
                            .then_inc(h_loaded[u], 16)

        def spread_over(t, n):
            return t.rearrange("p (b o) -> p b o", o=1).broadcast_to([t.shape[0], t.shape[1], n])

        def per_block(t):
            return t.rearrange("p (o d) -> p o d", o=1).broadcast_to([P, BLOCKS, t.shape[1]])

        @block.vector
        def _(dve):
            V = nc.vector

            def chain(name, base=0):
                n = [0]

                def step(instruction):
                    n[0] += 1
                    instruction.then_inc(name, 1)
                    dve.wait_ge(name, base + n[0])
                return step

            B1 = BLOCKS + 1
            did = chain(prep_dve)
            V.memset(z[:, :, :, 2 * D:ZW], 1.0)
            V.memset(hx[:, :, D:HW], 1.0)
            V.memset(total[:, :, :], 0.0).then_inc(total_ready, 1)
            V.memset(max_now[:, :], LOW).then_inc(max_now_ready, 1)
            V.memset(ones[:, :], 1.0)
            dve.wait_ge(s_iota, 2)
            V.tensor_copy(iota_row[:, :], iota_i[:, :])
            did(V.tensor_copy(iota_p[:, :], iota_pi[:, :]))
            V.tensor_scalar(limits[:, :], iota_row[:, 0:B1], float(P), None, ALU.mult)
            V.tensor_scalar(limit_p[:, :], iota_p[:, :], float(P), None, ALU.mult)
            V.tensor_scalar(shift_a[:, :], iota_row[:, 0:P], 1.0, None, ALU.add)
            V.tensor_scalar(shift_b[:, :], iota_row[:, 0:P], -1.0, None, ALU.add)
            V.tensor_scalar(earlier[:, :], iota_row[:, 0:P], iota_p[:, 0:1], None, ALU.is_gt)
            did(V.tensor_scalar(ident[:, :], iota_row[:, 0:P], iota_p[:, 0:1], None, ALU.is_equal))
            V.tensor_scalar(next_less[:, :], shift_a[:, :], iota_p[:, 0:1], None, ALU.is_equal)
            V.tensor_scalar(less_prev[:, :], shift_b[:, :], iota_p[:, 0:1], None, ALU.is_equal)
            did(V.tensor_scalar(is_later[:, :], iota_p[:, 0:1].broadcast_to([P, P]), 0.0, float(P), ALU.is_gt, ALU.mult))
            V.tensor_tensor(next_less[:, :], next_less[:, :], ident[:, :], ALU.subtract)
            V.tensor_tensor(less_prev[:, :], ident[:, :], less_prev[:, :], ALU.subtract)
            dve.wait_ge(s_dst, 16)
            samples = dst_all[:, :].rearrange("p (m c) -> p c m", c=SAMPLE)[:, 0:1, :]
            did(V.tensor_tensor(below[:, :, :], samples.broadcast_to([P, B1, BLOCKS]),
                                spread_over(limits[:, :], BLOCKS), ALU.is_lt))
            V.tensor_reduce(coarse[:, :], below[:, :, :], AX, ALU.add).then_inc(coarse_ready, 1)
            dve.wait_ge(pe_prep, 1)
            did(V.tensor_scalar(row_f[0:B1, :], bank[0][0:B1, 0:1], -1.0, 0.0, ALU.add, ALU.max))
            V.tensor_copy(row_i[0:B1, :], row_f[0:B1, :]).then_inc(row_ready, 1)
            dve.wait_ge(s_window, 16)
            did(V.tensor_scalar(fine[0:B1, :], window[0:B1, :], limit_p[0:B1, 0:1], None, ALU.is_lt))
            did(V.tensor_reduce(fine_n[0:B1, :], fine[0:B1, :], AX, ALU.add))
            V.scalar_tensor_tensor(start_col[0:B1, :], row_f[0:B1, :], float(SAMPLE), fine_n[0:B1, :],
                                   ALU.mult, ALU.add).then_inc(start_ready, 1)
            dve.wait_ge(pe_prep, 2)
            did(V.tensor_scalar(n_edges[0:BLOCKS, :], bank[1][0:BLOCKS, 0:1], float(C - 1), None, ALU.add))
            did(V.tensor_copy(n_i[0:BLOCKS, :], n_edges[0:BLOCKS, :]))
            did(V.tensor_scalar(n_shifted[0:BLOCKS, :], n_i[0:BLOCKS, :], LOG_C, None, ALU.arith_shift_right))
            V.tensor_scalar(n_steps[0:BLOCKS, :], n_shifted[0:BLOCKS, :], 1.0, None, ALU.max).then_inc(n_steps_ready, 1)
            dve.wait_ge(pe_prep, 3)
            did(V.tensor_copy(first_step[0:BLOCKS, :], bank[2][0:BLOCKS, 0:1]))
            V.scalar_tensor_tensor(base[0:BLOCKS, :], first_step[0:BLOCKS, :], -float(C), start_col[0:BLOCKS, :],
                                   ALU.mult, ALU.add).then_inc(base_ready, 1)
            V.tensor_scalar(begun[0:BLOCKS, :], iota_row[0:BLOCKS, :], first_step[0:BLOCKS, 0:1], None,
                            ALU.is_ge).then_inc(begun_ready, 1)
            dve.wait_ge(pe_prep, 4)
            V.tensor_copy(base_step[0:BLOCKS, :], bank[3][0:BLOCKS, 0:1]).then_inc(base_step_ready, 1)
            V.tensor_scalar(at_c[:, :], iota_row[0:1, :], float(C), None, ALU.mult).then_inc(prep_dve2, 1)
            dve.wait_ge(pe_prep, 5)
            dve.wait_ge(prep_dve2, 1)
            did(V.tensor_tensor(at_f[:, :], bank[4][0:1, 0:STEPS], at_c[:, :], ALU.add))
            did(V.tensor_scalar(at_c[:, :], at_f[:, :], float(E), None, ALU.min))
            V.tensor_copy(step_edge[:, :], at_c[:, :])
            dve.wait_ge(pe_prep, 6)
            did(V.tensor_copy(node_0[:, :], bank[5][:, 0:STEPS]))
            did(V.tensor_scalar(at_f[:, :], node_0[0:1, :], 1.0 / P, None, ALU.mult))
            V.tensor_copy(step_block[:, :], at_f[:, :]).then_inc(s_table, 1)
            did(V.tensor_tensor(same[:, 1:STEPS], node_0[:, 1:STEPS], node_0[:, 0:STEPS - 1], ALU.is_equal))
            V.memset(cap[:, 0:1], LOWER)
            did(V.tensor_scalar(cap[:, 1:STEPS], same[:, 1:STEPS], -2 * LOWER, LOWER, ALU.mult, ALU.add))

            def norm(n, norms_done, src, finish):
                did = chain(norm_dve, norms_done)
                did(V.tensor_reduce(stat[:, :], src, AX, ALU.add))
                did(V.tensor_scalar(spread[:, :], stat[:, :], 1.0 / D, None, ALU.mult))
                did(V.tensor_tensor(work[:, :, :], src, spread_over(spread[:, :], D), ALU.subtract))
                did(V.tensor_tensor(new[:, :, :], work[:, :, :], work[:, :, :], ALU.mult))
                did(V.tensor_reduce(stat[:, :], new[:, :, :], AX, ALU.add))
                V.tensor_scalar(spread[:, :], stat[:, :], 1.0 / D, EPS, ALU.mult, ALU.add).then_inc(variance_ready, 1)
                dve.wait_ge(deviation_ready, n + 1)
                did(V.reciprocal(inverse[:, :], deviation[:, :]))
                did(V.tensor_tensor(work[:, :, :], work[:, :, :], spread_over(inverse[:, :], D), ALU.mult))
                finish(did)

            def finish_first(did):
                V.tensor_scalar(hx[:, :, 0:D], work[:, :, :], 0.0, None, ALU.max).then_inc(h_ready, 1)

            def finish_layer(l):
                def finish(did):
                    dve.wait_ge(s_norm, (l + 1) * 32)
                    did(V.tensor_tensor(new[:, :, :], work[:, :, :], per_block(gamma_sb[:, :]), ALU.mult))
                    V.tensor_tensor(hx[:, :, 0:D], new[:, :, :], per_block(beta_sb[:, :]), ALU.add).then_inc(h_ready, 1)
                return finish

            def keep_qq(n):
                with dve.Fori(0, GROUPS) as g:
                    dve.wait_ge(qq_done, n * GROUPS + g + 1)
                    for k, i in enumerate(range(0, NG, 3)):
                        m = min(3, NG - i)
                        last = V.tensor_copy(qq_all[:, bass.ds(g * NG + i, m), :],
                                             bank[2 + k][:, 0:m * ZW].rearrange("p (i d) -> p i d", i=m))
                    last.then_inc(qq_ready, 1)

            def rel_of(l, r, s, u):
                dve.wait_ge(pair_loaded[u], (l * ROUNDS + r + 1) * 16)
                dst = pair[:, u, :].rearrange("p (j c) -> p j c", c=2)[:, :, 1]
                V.tensor_scalar(rel[:, u, :], dst, node_0[:, bass.ds(s, 1)], None, ALU.subtract).then_inc(rel_ready, 1)

            def at_node_of(l, s, u):
                dve.wait_ge(dst_row_ready, l * STEPS + s + 1)
                V.tensor_scalar(at_node[:, u % 2, :], dst_row[:, 0:C], iota_p[:, 0:1], None, ALU.is_equal)\
                    .then_inc(at_node_ready, 1)

            def alpha_of(l, r, s, u):
                dve.wait_ge(q_edge_ready, l * STEPS + s + 1)
                dve.wait_ge(edge_loaded[u], (l * ROUNDS + r + 1) * 32)
                dve.wait_ge(h_loaded[u], (l * ROUNDS + r + 1) * 16 * TILES)
                for j in range(TILES):
                    last = V.tensor_tensor_reduce(scratch_z[:, j, :], q_edge[j // 2][:, (j % 2) * 256:(j % 2) * 256 + ZW], z[:, u, j, :],
                                                  1.0, 0.0, ALU.mult, ALU.add, alpha[:, u, j:j + 1])
                last.then_inc(alpha_ready, 1)

            def step(l, r, s, u, ahead):
                g = l * STEPS + s
                before, v = (u - 1) % SLOTS, (u + 1) % SLOTS
                nr = r + (u + 1) // SLOTS
                if ahead:
                    rel_of(l, nr, s + 1, v)
                dve.wait_ge(max_now_ready, g + 1)
                V.tensor_scalar(max_before[:, u:u + 1], max_now[:, before:before + 1], cap[:, bass.ds(s, 1)], None, ALU.min)\
                    .then_inc(max_before_ready, 1)
                dve.wait_ge(alpha_row_ready, g + 1)
                dve.wait_ge(barred_ready, g + 1)
                dve.sem_inc(passed_dve, 1)
                V.tensor_tensor_reduce(scratch_c[:, :], alpha_row[:, 0:C], barred[:, u % 2, :], 1.0, LOW, ALU.add, ALU.max,
                                       max_step[:, u:u + 1]).then_inc(max_step_ready, 1)
                dve.wait_ge(max_before_ready, g + 1)
                dve.wait_ge(max_step_ready, g + 1)
                V.tensor_tensor(max_now[:, u:u + 1], max_before[:, u:u + 1], max_step[:, u:u + 1], ALU.max)\
                    .then_inc(max_now_ready, 1)
                if ahead:
                    at_node_of(l, s + 1, v)
                dve.wait_ge(max_now_ready, g + 2)
                V.tensor_tensor(max_fell[:, u:u + 1], max_before[:, u:u + 1], max_now[:, u:u + 1], ALU.subtract)\
                    .then_inc(max_fell_ready, 1)
                dve.wait_ge(edge_max_ready, g + 1)
                V.tensor_tensor(less_max[:, u, :], alpha[:, u, :], edge_max[:, 0:TILES], ALU.subtract)\
                    .then_inc(less_max_ready, 1)
                dve.wait_ge(prob_ready, g + 1)
                for j in range(TILES):
                    V.tensor_scalar(weigh[:, u % 2, j, :], iota_row[:, 0:P], rel[:, u, j:j + 1], prob[:, u, j:j + 1],
                                    ALU.is_equal, ALU.mult).then_inc(weigh_ready, 1)
                if ahead:
                    alpha_of(l, nr, s + 1, v)
                else:
                    dve.wait_ge(total_kept, (g - SLOTS + 1) * 16)
                dve.wait_ge(sums_ready, g + 1)
                dve.wait_ge(rescale_ready, g + 1)
                dve.wait_ge(total_ready, g + 1)
                V.scalar_tensor_tensor(total[:, u, :], total[:, before, :], rescale[:, u:u + 1], sums[u % 2][:, 0:ZW],
                                       ALU.mult, ALU.add).then_inc(total_ready, 1)

            def edge_phase(l):
                rel_of(l, 0, 0, 0)
                at_node_of(l, 0, 0)
                alpha_of(l, 0, 0, 0)
                with dve.Fori(0, ROUNDS - 1) as r:
                    for u in range(SLOTS):
                        step(l, r, r * SLOTS + u, u, True)
                for u in range(SLOTS):
                    step(l, ROUNDS - 1, STEPS - SLOTS + u, u, u < SLOTS - 1)

            def outputs(l):
                did = chain(mean_dve, l * MEAN_OPS)
                dve.wait_ge(total_kept, (l + 1) * STEPS * 16)
                weight = u_all[:, :, 2 * D:ZW].rearrange("p b o -> p (b o)")
                V.tensor_scalar(hx[:, :, D + 1:HW].rearrange("p b o -> p (b o)"), weight, 0.0, None, ALU.is_gt)
                did(V.tensor_scalar(stat[:, :], weight, 1e-30, None, ALU.max))
                V.reciprocal(inverse[:, :], stat[:, :]).then_inc(weights_ready, 1)
                dve.wait_ge(weights_ready, l + 1)
                dve.sem_inc(passed_dve, 1)
                with dve.Fori(0, GROUPS) as g:
                    V.tensor_tensor(mean_g[:, :, :], u_all[:, bass.ds(g * NG, NG), 0:2 * D],
                                    spread_over(inverse[:, bass.ds(g * NG, NG)], 2 * D), ALU.mult).then_inc(mean_ready, 1)
                    dve.wait_ge(ht_done, l * GROUPS + g + 1)
                    V.tensor_copy(ht[:, 0:4, :], bank[2][0:HW, :].rearrange("p (i n) -> p i n", n=P))
                    V.tensor_copy(ht[:, 4:NG, :], bank[3][0:HW, 0:(NG - 4) * P].rearrange("p (i n) -> p i n", n=P))\
                        .then_inc(ht_ready, 1)

            dve.wait_ge(s_x, 16)
            norm(0, 0, x_in[:, :, :], finish_first)
            keep_qq(0)
            with dve.Fori(0, LAYERS - 1) as l:
                edge_phase(l)
                outputs(l)
                dve.wait_ge(new_ready, (l + 1) * GROUPS)
                norm(l + 1, NORM_OPS + l * (NORM_OPS + 1), new[:, :, :], finish_layer(l))
                keep_qq(l + 1)
            edge_phase(LAYERS - 1)
            outputs(LAYERS - 1)
            dve.wait_ge(new_ready, LAYERS * GROUPS)
            did = chain(last_dve)
            did(V.tensor_reduce(stat[:, :], new[:, :, :], AX, ALU.max))
            V.tensor_tensor(work[:, :, :], new[:, :, :], spread_over(stat[:, :], D), ALU.subtract).then_inc(shifted_ready, 1)
            dve.wait_ge(exp_ready, 1)
            V.tensor_reduce(spread[:, :], exps[:, :, :], AX, ALU.add).then_inc(sum_ready, 1)
            dve.wait_ge(log_ready, 1)
            dve.wait_ge(shifted_ready, 1)
            did(V.tensor_tensor(new[:, :, :], work[:, :, :], spread_over(deviation[:, :], D), ALU.subtract))
            V.tensor_tensor(work[:, :, :], new[:, :, :], x_in[:, :, :], ALU.add).then_inc(out_ready, 1)

        @block.scalar
        def _(act):
            A = nc.scalar

            def barred_of(g, u):
                act.wait_ge(at_node_ready, g + 1)
                A.activation(barred[:, u % 2, :], at_node[:, u % 2, :], ACT.Copy, bias=LOW, scale=-LOW)\
                    .then_inc(barred_ready, 1)

            def step(g, u, ahead):
                if ahead:
                    barred_of(g + 1, u + 1)
                act.wait_ge(max_fell_ready, g + 1)
                A.activation(rescale[:, u:u + 1], max_fell[:, u:u + 1], ACT.Exp).then_inc(rescale_ready, 1)
                act.wait_ge(less_max_ready, g + 1)
                A.activation(prob[:, u, :], less_max[:, u, :], ACT.Exp).then_inc(prob_ready, 1)

            def edge_phase(l):
                barred_of(l * STEPS, 0)
                with act.Fori(0, ROUNDS - 1) as r:
                    for u in range(SLOTS):
                        step(l * STEPS + r * SLOTS + u, u, True)
                for u in range(SLOTS):
                    step(l * STEPS + STEPS - SLOTS + u, u, u < SLOTS - 1)

            def make_qq(n):
                act.wait_ge(h_ready, n + 1)
                act.wait_ge(wqk_done, n + 1)
                A.activation(wqk[:, :], bank[7][0:D + 1, 0:ZW], ACT.Copy, scale=float(D) ** -0.5).then_inc(wqk_ready, 1)
                with act.Fori(0, GROUPS) as g:
                    A.activation(hx_g[:, :, 0:D + 1], hx[:, bass.ds(g * NG, NG), 0:D + 1], ACT.Copy).then_inc(hx_g_ready, 1)
                    act.wait_ge(qt_done, n * GROUPS + g + 1)
                    A.activation(ht[0:D + 1, 0:4, :], bank[0][0:D + 1, :].rearrange("p (i n) -> p i n", n=P), ACT.Copy)
                    A.activation(ht[0:D + 1, 4:NG, :], bank[1][0:D + 1, 0:(NG - 4) * P].rearrange("p (i n) -> p i n", n=P),
                                 ACT.Copy).then_inc(qt_ready, 1)

            def outputs(l):
                act.wait_ge(weights_ready, l + 1)
                with act.Fori(0, GROUPS) as g:
                    A.activation(hx_g[:, :, :], hx[:, bass.ds(g * NG, NG), :], ACT.Copy).then_inc(hx_h_ready, 1)
                    act.wait_ge(zt_done, l * GROUPS + g + 1)
                    A.activation(zt[:, 0:4, :], bank[0][:, :].rearrange("p (i n) -> p i n", n=P), ACT.Copy)
                    A.activation(zt[:, 4:NG, :], bank[1][:, 0:(NG - 4) * P].rearrange("p (i n) -> p i n", n=P),
                                 ACT.Copy).then_inc(zt_ready, 1)
                    act.wait_ge(new_done, l * GROUPS + g + 1)
                    A.activation(new[:, bass.ds(g * NG, NG), :], bank[4][:, 0:NG * D].rearrange("p (i d) -> p i d", d=D),
                                 ACT.Relu).then_inc(new_ready, 1)

            def norm(n):
                act.wait_ge(variance_ready, n + 1)
                A.activation(deviation[:, :], spread[:, :], ACT.Sqrt).then_inc(deviation_ready, 1)

            norm(0)
            make_qq(0)
            with act.Fori(0, LAYERS - 1) as l:
                edge_phase(l)
                outputs(l)
                norm(l + 1)
                make_qq(l + 1)
            edge_phase(LAYERS - 1)
            outputs(LAYERS - 1)
            act.wait_ge(shifted_ready, 1)
            A.activation(exps[:, :, :], work[:, :, :], ACT.Exp).then_inc(exp_ready, 1)
            act.wait_ge(sum_ready, 1)
            A.activation(deviation[:, :], spread[:, :], ACT.Ln).then_inc(log_ready, 1)

        @block.tensor
        def _(pe):
            T = nc.tensor
            B1 = BLOCKS + 1

            def product(out, left, right, start=True, stop=True):
                return T.matmul(out, left, right, start=start, stop=stop)

            pe.wait_ge(coarse_ready, 1)
            product(bank[0][0:B1, 0:1], coarse[:, :], ones[:, :]).then_inc(pe_prep, 1)
            pe.wait_ge(start_ready, 1)
            product(bank[1][0:BLOCKS, 0:1], next_less[0:B1, 0:BLOCKS], start_col[0:B1, :]).then_inc(pe_prep, 1)
            pe.wait_ge(n_steps_ready, 1)
            product(bank[2][0:BLOCKS, 0:1], earlier[0:BLOCKS, 0:BLOCKS], n_steps[0:BLOCKS, :]).then_inc(pe_prep, 1)
            pe.wait_ge(base_ready, 1)
            product(bank[3][0:BLOCKS, 0:1], less_prev[0:BLOCKS, 0:BLOCKS], base[0:BLOCKS, :]).then_inc(pe_prep, 1)
            pe.wait_ge(base_step_ready, 1)
            pe.wait_ge(begun_ready, 1)
            product(bank[4][0:1, 0:STEPS], base_step[0:BLOCKS, :], begun[0:BLOCKS, :]).then_inc(pe_prep, 1)
            product(bank[5][:, 0:STEPS], is_later[0:BLOCKS, :], begun[0:BLOCKS, :]).then_inc(pe_prep, 1)

            def dst_row_of(g, u):
                pe.wait_ge(rel_ready, g + 1)
                for j in range(TILES):
                    last = T.transpose(dst_row[:, j * P:(j + 1) * P], rel[:, u, j:j + 1].broadcast_to([P, P]), ident[:, :])
                last.then_inc(dst_row_ready, 1)

            def q_edge_of(l, r, g, u):
                pe.wait_ge(at_node_ready, g + 1)
                pe.wait_ge(edge_loaded[u], (l * ROUNDS + r + 1) * 32)
                for j in range(TILES):
                    last = product(q_edge[j // 2][:, (j % 2) * 256:(j % 2) * 256 + ZW],
                                   at_node[:, u % 2, j * P:(j + 1) * P], qq[:, u, :])
                last.then_inc(q_edge_ready, 1)

            def step(l, r, s, u, ahead):
                g = l * STEPS + s
                v, nr = (u + 1) % SLOTS, r + (u + 1) // SLOTS
                pe.wait_ge(alpha_ready, g + 1)
                for j in range(TILES):
                    last = T.transpose(alpha_row[:, j * P:(j + 1) * P], alpha[:, u, j:j + 1].broadcast_to([P, P]), ident[:, :])
                last.then_inc(alpha_row_ready, 1)
                if ahead:
                    dst_row_of(g + 1, v)
                pe.wait_ge(max_now_ready, g + 2)
                for j in range(TILES):
                    last = product(edge_max[:, j:j + 1], at_node[:, u % 2, j * P:(j + 1) * P], max_now[:, u:u + 1])
                last.then_inc(edge_max_ready, 1)
                if ahead:
                    q_edge_of(l, nr, g + 1, v)
                for j in range(TILES):
                    pe.wait_ge(weigh_ready, g * TILES + j + 1)
                    last = product(sums[u % 2][:, 0:ZW], weigh[:, u % 2, j, :], z[:, u, j, :], j == 0, j == TILES - 1)
                last.then_inc(sums_ready, 1)

            def edge_phase(l):
                dst_row_of(l * STEPS, 0)
                q_edge_of(l, 0, l * STEPS, 0)
                with pe.Fori(0, ROUNDS - 1) as r:
                    for u in range(SLOTS):
                        step(l, r, r * SLOTS + u, u, True)
                for u in range(SLOTS):
                    step(l, ROUNDS - 1, STEPS - SLOTS + u, u, u < SLOTS - 1)

            def make_qq(n):
                pe.wait_ge(weights_in, (n + 1) * 32)
                product(bank[7][0:D + 1, 0:ZW], wq_sb[:, :], wk_sb[:, :]).then_inc(wqk_done, 1)
                pe.wait_ge(wqk_ready, n + 1)
                pe.sem_inc(passed_pe, 1)
                with pe.Fori(0, GROUPS) as g:
                    pe.wait_ge(hx_g_ready, n * GROUPS + g + 1)
                    for i in range(NG):
                        last = T.transpose(bank[i // 4][0:D + 1, (i % 4) * P:(i % 4 + 1) * P],
                                           hx_g[:, i, 0:D + 1], ident[:, :])
                    last.then_inc(qt_done, 1)
                    pe.wait_ge(qt_ready, n * GROUPS + g + 1)
                    for i in range(NG):
                        last = product(bank[2 + i // 3][:, (i % 3) * ZW:(i % 3 + 1) * ZW], ht[0:D + 1, i, :], wqk[:, :])
                    last.then_inc(qq_done, 1)
                    pe.wait_ge(qq_ready, n * GROUPS + g + 1)

            def outputs(l):
                pe.wait_ge(s_w, (l + 1) * 32)
                pe.sem_inc(passed_pe, 1)
                with pe.Fori(0, GROUPS) as g:
                    pe.wait_ge(mean_ready, l * GROUPS + g + 1)
                    for i in range(NG):
                        last = T.transpose(bank[i // 4][:, (i % 4) * P:(i % 4 + 1) * P],
                                           mean_g[:, i, :], ident[:, :])
                    last.then_inc(zt_done, 1)
                    pe.wait_ge(hx_h_ready, l * GROUPS + g + 1)
                    for i in range(NG):
                        last = T.transpose(bank[2 + i // 4][0:HW, (i % 4) * P:(i % 4 + 1) * P],
                                           hx_g[:, i, :], ident[:, :])
                    last.then_inc(ht_done, 1)
                    pe.wait_ge(zt_ready, l * GROUPS + g + 1)
                    pe.wait_ge(ht_ready, l * GROUPS + g + 1)
                    for i in range(NG):
                        product(bank[4][:, i * D:(i + 1) * D], zt[:, i, :], wv_sb[:, :], True, False)
                        last = product(bank[4][:, i * D:(i + 1) * D], ht[:, i, :], ws_sb[:, :], False, True)
                    last.then_inc(new_done, 1)
                    pe.wait_ge(new_ready, l * GROUPS + g + 1)

            make_qq(0)
            with pe.Fori(0, LAYERS - 1) as l:
                edge_phase(l)
                outputs(l)
                make_qq(l + 1)
            edge_phase(LAYERS - 1)
            outputs(LAYERS - 1)


def kernel(x, src, dst, edge_attr_64, L0_gnn_Wq, L0_gnn_bq, L0_gnn_Wk, L0_gnn_bk, L0_gnn_Wv, L0_gnn_bv, L0_gnn_We,
           L0_gnn_Ws, L0_gnn_bs, L0_gnn_ln_gamma, L0_gnn_ln_beta):
    import concourse.bacc as bacc
    from concourse.bass_utils import run_bass_kernel_spmd

    nc = bacc.Bacc("TRN2", target_bir_lowering=False, num_devices=1)
    src, dst, edge_attr = np.asarray(src), np.asarray(dst), np.asarray(edge_attr_64)
    wq, wk, wv, we, ws = map(np.asarray, (L0_gnn_Wq, L0_gnn_Wk, L0_gnn_Wv, L0_gnn_We, L0_gnn_Ws))
    bq, bk, bv, bs = (np.asarray(b)[:, None, :] for b in (L0_gnn_bq, L0_gnn_bk, L0_gnn_bv, L0_gnn_bs))

    def turned(a):
        return a.transpose(0, 2, 1)

    dst_padded = np.concatenate([dst, np.full(EPAD - E, FAR, dst.dtype)])
    src_padded = np.concatenate([src, np.zeros(EPAD - E, src.dtype)])
    laid = {
        "x": np.concatenate([np.asarray(x), np.zeros((NPAD - N, D), np.float32)]),
        "ends": np.stack([src_padded, dst_padded], axis=1),
        "dst_rows": dst_padded.reshape(-1, SAMPLE),
        "edge_attr": np.concatenate([edge_attr, np.zeros((EPAD - E, D), np.float32)]),
        "wq_t": np.concatenate([turned(wq), turned(bq)], axis=2),
        "w_keys": np.concatenate([turned(wk), turned(we), turned(bk)], axis=2),
        "w_values": np.concatenate([wv, we], axis=1),
        "w_skip": np.concatenate([ws, bs, bv], axis=1),
        "gamma": np.asarray(L0_gnn_ln_gamma),
        "beta": np.asarray(L0_gnn_ln_beta),
    }
    laid = {f"in_{name}": np.ascontiguousarray(a) for name, a in laid.items()}
    args = [nc.dram_tensor(name, a.shape, mybir.dt.from_np(a.dtype), kind="ExternalInput").ap() for name, a in laid.items()]
    out = nc.dram_tensor("out_0", (N, D), F32, kind="ExternalOutput").ap()
    program(nc, *args, out)
    return run_bass_kernel_spmd(nc, [laid], core_ids=[0]).results[0]["out_0"]
```
